# Optimizing a Trainium2 kernel written in Bass

```python
import numpy as np
import jax
import jax.numpy as jnp

def _softmax(x, axis=-1):
    return jax.nn.softmax(x, axis=axis)

def _gelu(x):
    return jax.nn.gelu(x, approximate=True)

def _silu(x):
    return jax.nn.silu(x)

def _sigmoid(x):
    return jax.nn.sigmoid(x)

def _layernorm(x, axis=-1, eps=1e-05):
    m = jnp.mean(x, axis=axis, keepdims=True)
    v = jnp.var(x, axis=axis, keepdims=True)
    return (x - m) / jnp.sqrt(v + eps)

def _scatter_add(tgt, idx, src, axis=0):
    return tgt.at[idx].add(src)

def _segment_sum(src, seg, n):
    return jax.ops.segment_sum(src, seg, n)
kernel_name = 'mk_dlrm_tower_d1_rec_r8_3e640b'

def setup_inputs(seed: int=0):
    np.random.seed(seed)
    _w = jnp.asarray

    def _rec_inputs():
        import jax
        import jax.numpy as jnp
        _tk = jax.random.key(seed)
        dense_ctx = jax.random.normal(jax.random.fold_in(_tk, 190), (2048, 16), jnp.float32)
        ids = jnp.stack([jax.random.randint(jax.random.fold_in(_tk, 200 + f), (2048,), 0, v, jnp.int32) for f, v in enumerate([1250, 1250, 1000, 12500, 125000, 1250, 1000, 1250, 1250, 125000, 1000, 12500, 1000, 1000, 125000, 1000, 1000, 12500, 1250, 1000, 12500, 1000, 1250, 1000, 1000, 1000, 1250, 1250, 12500, 12500, 1000, 1000])], axis=1)
        tbl_0 = 0.05 * jax.random.normal(jax.random.fold_in(_tk, 500 + 0), (1250, 64), jnp.float32)
        tbl_1 = 0.05 * jax.random.normal(jax.random.fold_in(_tk, 500 + 1), (1250, 64), jnp.float32)
        tbl_2 = 0.05 * jax.random.normal(jax.random.fold_in(_tk, 500 + 2), (1000, 64), jnp.float32)
        tbl_3 = 0.05 * jax.random.normal(jax.random.fold_in(_tk, 500 + 3), (12500, 64), jnp.float32)
        tbl_4 = 0.05 * jax.random.normal(jax.random.fold_in(_tk, 500 + 4), (125000, 64), jnp.float32)
        tbl_5 = 0.05 * jax.random.normal(jax.random.fold_in(_tk, 500 + 5), (1250, 64), jnp.float32)
        tbl_6 = 0.05 * jax.random.normal(jax.random.fold_in(_tk, 500 + 6), (1000, 64), jnp.float32)
        tbl_7 = 0.05 * jax.random.normal(jax.random.fold_in(_tk, 500 + 7), (1250, 64), jnp.float32)
        tbl_8 = 0.05 * jax.random.normal(jax.random.fold_in(_tk, 500 + 8), (1250, 64), jnp.float32)
        tbl_9 = 0.05 * jax.random.normal(jax.random.fold_in(_tk, 500 + 9), (125000, 64), jnp.float32)
        tbl_10 = 0.05 * jax.random.normal(jax.random.fold_in(_tk, 500 + 10), (1000, 64), jnp.float32)
        tbl_11 = 0.05 * jax.random.normal(jax.random.fold_in(_tk, 500 + 11), (12500, 64), jnp.float32)
        tbl_12 = 0.05 * jax.random.normal(jax.random.fold_in(_tk, 500 + 12), (1000, 64), jnp.float32)
        tbl_13 = 0.05 * jax.random.normal(jax.random.fold_in(_tk, 500 + 13), (1000, 64), jnp.float32)
        tbl_14 = 0.05 * jax.random.normal(jax.random.fold_in(_tk, 500 + 14), (125000, 64), jnp.float32)
        tbl_15 = 0.05 * jax.random.normal(jax.random.fold_in(_tk, 500 + 15), (1000, 64), jnp.float32)
        tbl_16 = 0.05 * jax.random.normal(jax.random.fold_in(_tk, 500 + 16), (1000, 64), jnp.float32)
        tbl_17 = 0.05 * jax.random.normal(jax.random.fold_in(_tk, 500 + 17), (12500, 64), jnp.float32)
        tbl_18 = 0.05 * jax.random.normal(jax.random.fold_in(_tk, 500 + 18), (1250, 64), jnp.float32)
        tbl_19 = 0.05 * jax.random.normal(jax.random.fold_in(_tk, 500 + 19), (1000, 64), jnp.float32)
        tbl_20 = 0.05 * jax.random.normal(jax.random.fold_in(_tk, 500 + 20), (12500, 64), jnp.float32)
        tbl_21 = 0.05 * jax.random.normal(jax.random.fold_in(_tk, 500 + 21), (1000, 64), jnp.float32)
        tbl_22 = 0.05 * jax.random.normal(jax.random.fold_in(_tk, 500 + 22), (1250, 64), jnp.float32)
        tbl_23 = 0.05 * jax.random.normal(jax.random.fold_in(_tk, 500 + 23), (1000, 64), jnp.float32)
        tbl_24 = 0.05 * jax.random.normal(jax.random.fold_in(_tk, 500 + 24), (1000, 64), jnp.float32)
        tbl_25 = 0.05 * jax.random.normal(jax.random.fold_in(_tk, 500 + 25), (1000, 64), jnp.float32)
        tbl_26 = 0.05 * jax.random.normal(jax.random.fold_in(_tk, 500 + 26), (1250, 64), jnp.float32)
        tbl_27 = 0.05 * jax.random.normal(jax.random.fold_in(_tk, 500 + 27), (1250, 64), jnp.float32)
        tbl_28 = 0.05 * jax.random.normal(jax.random.fold_in(_tk, 500 + 28), (12500, 64), jnp.float32)
        tbl_29 = 0.05 * jax.random.normal(jax.random.fold_in(_tk, 500 + 29), (12500, 64), jnp.float32)
        tbl_30 = 0.05 * jax.random.normal(jax.random.fold_in(_tk, 500 + 30), (1000, 64), jnp.float32)
        tbl_31 = 0.05 * jax.random.normal(jax.random.fold_in(_tk, 500 + 31), (1000, 64), jnp.float32)
        _rk = jax.random.fold_in(_tk, 7)
        W_top1 = 0.0441942 * jax.random.normal(jax.random.fold_in(_tk, 801), (512, 512), jnp.float32)
        W_top2 = 0.0441942 * jax.random.normal(jax.random.fold_in(_tk, 802), (512, 256), jnp.float32)
        W_top3 = 0.0625 * jax.random.normal(jax.random.fold_in(_tk, 803), (256, 1), jnp.float32)
        b_top1 = jnp.zeros((512,), jnp.float32)
        b_top2 = jnp.zeros((256,), jnp.float32)
        return (dense_ctx, ids, tbl_0, tbl_1, tbl_2, tbl_3, tbl_4, tbl_5, tbl_6, tbl_7, tbl_8, tbl_9, tbl_10, tbl_11, tbl_12, tbl_13, tbl_14, tbl_15, tbl_16, tbl_17, tbl_18, tbl_19, tbl_20, tbl_21, tbl_22, tbl_23, tbl_24, tbl_25, tbl_26, tbl_27, tbl_28, tbl_29, tbl_30, tbl_31, W_top1, b_top1, W_top2, b_top2, W_top3)
    dense_ctx, ids, tbl_0, tbl_1, tbl_2, tbl_3, tbl_4, tbl_5, tbl_6, tbl_7, tbl_8, tbl_9, tbl_10, tbl_11, tbl_12, tbl_13, tbl_14, tbl_15, tbl_16, tbl_17, tbl_18, tbl_19, tbl_20, tbl_21, tbl_22, tbl_23, tbl_24, tbl_25, tbl_26, tbl_27, tbl_28, tbl_29, tbl_30, tbl_31, W_top1, b_top1, W_top2, b_top2, W_top3 = _rec_inputs()

    def _L0_rec_setup():
        import jax, jax.numpy as jnp
        import numpy as np
        BATCH = 1024
        NUM_FIELDS = 32
        EMBED_DIM = 64
        NUM_IX = NUM_FIELDS * (NUM_FIELDS - 1) // 2
        key = jax.random.key(seed)
        kx, kk = jax.random.split(key)
        x = jax.random.normal(kx, (BATCH, NUM_FIELDS, EMBED_DIM), dtype=jnp.float32)
        fan = EMBED_DIM + EMBED_DIM
        limit = float(np.sqrt(6.0 / fan))
        kernel = jax.random.uniform(kk, (EMBED_DIM, NUM_IX, EMBED_DIM), dtype=jnp.float32, minval=-limit, maxval=limit)
        return {'x': x, 'kernel': kernel}
    _L0_rec_all = _L0_rec_setup()
    _L0_rec_in = {k: v for k, v in _L0_rec_all.items() if k in ('kernel',)}
    del _L0_rec_all
    return {'dense_ctx': dense_ctx, 'ids': ids, 'tbl_0': tbl_0, 'tbl_1': tbl_1, 'tbl_2': tbl_2, 'tbl_3': tbl_3, 'tbl_4': tbl_4, 'tbl_5': tbl_5, 'tbl_6': tbl_6, 'tbl_7': tbl_7, 'tbl_8': tbl_8, 'tbl_9': tbl_9, 'tbl_10': tbl_10, 'tbl_11': tbl_11, 'tbl_12': tbl_12, 'tbl_13': tbl_13, 'tbl_14': tbl_14, 'tbl_15': tbl_15, 'tbl_16': tbl_16, 'tbl_17': tbl_17, 'tbl_18': tbl_18, 'tbl_19': tbl_19, 'tbl_20': tbl_20, 'tbl_21': tbl_21, 'tbl_22': tbl_22, 'tbl_23': tbl_23, 'tbl_24': tbl_24, 'tbl_25': tbl_25, 'tbl_26': tbl_26, 'tbl_27': tbl_27, 'tbl_28': tbl_28, 'tbl_29': tbl_29, 'tbl_30': tbl_30, 'tbl_31': tbl_31, 'W_top1': W_top1, 'b_top1': b_top1, 'W_top2': W_top2, 'b_top2': b_top2, 'W_top3': W_top3, 'L0_rec_kernel': _L0_rec_in['kernel']}

def reference(dense_ctx, ids, tbl_0, tbl_1, tbl_2, tbl_3, tbl_4, tbl_5, tbl_6, tbl_7, tbl_8, tbl_9, tbl_10, tbl_11, tbl_12, tbl_13, tbl_14, tbl_15, tbl_16, tbl_17, tbl_18, tbl_19, tbl_20, tbl_21, tbl_22, tbl_23, tbl_24, tbl_25, tbl_26, tbl_27, tbl_28, tbl_29, tbl_30, tbl_31, W_top1, b_top1, W_top2, b_top2, W_top3, L0_rec_kernel):
    import jax
    import jax.numpy as jnp

    def _L0_rec_ref(x, kernel):
        import jax, jax.numpy as jnp
        import numpy as np
        BATCH = 1024
        NUM_FIELDS = 32
        EMBED_DIM = 64
        NUM_IX = NUM_FIELDS * (NUM_FIELDS - 1) // 2
        num_fields = x.shape[1]
        row, col = np.triu_indices(num_fields, k=1)
        p = x[:, row]
        q = x[:, col]
        out = jnp.einsum('bni,oni,bno->bn', p, kernel, q)
        return out
    e = jnp.stack([tbl_0[ids[:, 0]], tbl_1[ids[:, 1]], tbl_2[ids[:, 2]], tbl_3[ids[:, 3]], tbl_4[ids[:, 4]], tbl_5[ids[:, 5]], tbl_6[ids[:, 6]], tbl_7[ids[:, 7]], tbl_8[ids[:, 8]], tbl_9[ids[:, 9]], tbl_10[ids[:, 10]], tbl_11[ids[:, 11]], tbl_12[ids[:, 12]], tbl_13[ids[:, 13]], tbl_14[ids[:, 14]], tbl_15[ids[:, 15]], tbl_16[ids[:, 16]], tbl_17[ids[:, 17]], tbl_18[ids[:, 18]], tbl_19[ids[:, 19]], tbl_20[ids[:, 20]], tbl_21[ids[:, 21]], tbl_22[ids[:, 22]], tbl_23[ids[:, 23]], tbl_24[ids[:, 24]], tbl_25[ids[:, 25]], tbl_26[ids[:, 26]], tbl_27[ids[:, 27]], tbl_28[ids[:, 28]], tbl_29[ids[:, 29]], tbl_30[ids[:, 30]], tbl_31[ids[:, 31]]], axis=1)
    z = _L0_rec_ref(e, L0_rec_kernel)
    z = z.reshape(z.shape[0], -1)
    h = jnp.concatenate([z, dense_ctx], axis=1)
    h = jnp.maximum(h @ W_top1 + b_top1, 0.0)
    h = jnp.maximum(h @ W_top2 + b_top2, 0.0)
    y = h @ W_top3
    return y

_drawn_inputs = setup_inputs


def setup_inputs(seed=0):
    import zlib

    import numpy as np

    out = dict(_drawn_inputs(seed))
    spreads = {'b_top1': (0.0, 0.1), 'b_top2': (0.0, 0.1)}
    factors = {}
    for name, (base, spread) in spreads.items():
        noise = np.random.default_rng([zlib.crc32(name.encode()), seed]).standard_normal(out[name].shape)
        drawn = base * np.exp(spread * noise) if base else spread * noise
        out[name] = jnp.asarray(drawn.astype(out[name].dtype))
    for name, factor in factors.items():
        out[name] = (out[name] * factor).astype(out[name].dtype)
    return out
```

```python
from contextlib import ExitStack

import numpy as np

import concourse.bass as bass
from concourse import mybir

F32 = mybir.dt.float32
F32R = mybir.dt.float32r
I32 = mybir.dt.int32
U32 = mybir.dt.uint32
ALU = mybir.AluOpType
ACT = mybir.ActivationFunctionType

BATCH, FIELDS, DIM, DENSE = 2048, 32, 64, 16
H1, H2 = 512, 256
PAIRS = FIELDS * (FIELDS - 1) // 2
PHASES = FIELDS // 2
N = 256
SUBS = N // 128
TILES = BATCH // N
K_COLS = PAIRS * DIM
PIECE = 1024
PIECES = K_COLS // PIECE
Z_BLOCKS = (PAIRS + DENSE) // 128
H1_BLOCKS, H2_BLOCKS = H1 // 128, H2 // 128
MLP_STEPS = H1_BLOCKS + H2_BLOCKS + 1
MLP_AT = {n: n for n in range(MLP_STEPS)}

STAGE_SLOTS = 8
MOVING_SLOTS = 4
T_SLOTS = 2
PROD_SLOTS = 4
SUM_LAG = 3
K_SLOTS = 3


def plan():
    k_order, at = [], {}
    for m in range(PHASES):
        for k in range(m):
            for c in (2 * m, 2 * m + 1):
                for r in (2 * k, 2 * k + 1):
                    at[(r, c)] = len(k_order) * DIM
                    k_order.append((r, c))
        at[(2 * m, 2 * m + 1)] = len(k_order) * DIM
        k_order.append((2 * m, 2 * m + 1))

    items = []
    for m in range(PHASES):
        for k in range(0, m - 1, 2):
            chunks = [(at[(2 * kk, c)], 2 * DIM, c) for kk in (k, k + 1) for c in (2 * m, 2 * m + 1)]
            items.append({"m": m, "k": k, "tail": None, "chunks": chunks})
        if m % 2:
            chunks = [(at[(2 * m - 2, c)], 2 * DIM, c) for c in (2 * m, 2 * m + 1)]
            chunks += [(at[(2 * n, 2 * n + 1)], DIM, 2 * n + 1) for n in (m - 1, m)]
            items.append({"m": m, "k": m - 1, "tail": m // 2, "chunks": chunks})

    def pair_row(r, c):
        return r * (FIELDS - 1) - r * (r - 1) // 2 + c - r - 1

    z_rows = [None] * (PAIRS + DENSE)
    per_block = len(items) // Z_BLOCKS
    for i, item in enumerate(items):
        for q, (_, columns, c) in enumerate(item["chunks"]):
            row = 128 * (i // per_block) + 32 * q + 2 * (i % per_block)
            if columns == DIM:
                z_rows[row] = pair_row(c - 1, c)
                z_rows[row + 1] = PAIRS + 2 * item["tail"] + q - 2
            else:
                k = item["k"] + (q // 2 if item["tail"] is None else 0)
                z_rows[row] = pair_row(2 * k, c)
                z_rows[row + 1] = pair_row(2 * k + 1, c)
    assert sorted(z_rows) == list(range(PAIRS + DENSE))
    return [pair_row(r, c) for r, c in k_order], items, z_rows


K_ORDER, ITEM_LIST, Z_ROWS = plan()
ITEMS = len(ITEM_LIST)
ITEMS_PER_BLOCK = ITEMS // Z_BLOCKS
FIRST_ITEM = [next(i for i, x in enumerate(ITEM_LIST) if x["m"] >= m) for m in range(PHASES)]
LAST_ITEM = [max(i for i, x in enumerate(ITEM_LIST) if x["m"] == m | 1) for m in range(PHASES)]
TAIL_ITEM = [i for i, x in enumerate(ITEM_LIST) if x["tail"] is not None]
LAST_USE = [FIRST_ITEM[PHASES - 1] + k // 2 for k in range(PHASES - 1)] + [ITEMS - 1]

EARLY = 4
PREPARE = {i: [] for i in range(ITEMS + 1)}
for _p in range(EARLY, PHASES):
    PREPARE[max(LAST_ITEM[_p - MOVING_SLOTS] + 1, FIRST_ITEM[_p] - 6, _p - 3)].append((0, _p))
for _p in range(EARLY - 1):
    PREPARE[FIRST_ITEM[PHASES - 1] + 3 + _p].append((1, _p))
PREPARE[ITEMS].append((1, EARLY - 1))


def last_piece(i):
    return max(col + width - 1 for col, width, _ in ITEM_LIST[i]["chunks"]) // PIECE


K_FIRST = 12
K_LEAD = 16
K_AT = {i: [] for i in range(ITEMS)}
for _piece in range(K_FIRST, PIECES):
    _first = next(i for i in range(ITEMS) if last_piece(i) >= _piece)
    K_AT[max(0, _first - K_LEAD)].append(_piece)


def wait_count(engine, semaphore, count):
    if isinstance(count, int) and count <= 0:
        return
    engine.wait_ge(semaphore, count)


def dlrm_tower(nc, ids, tables, kernel, w1, b1, w2, b2, w3, dense, sel_in, ident_in, y_out):
    ctx = ExitStack()
    with ctx:
        def sb(name, shape, dt=F32):
            return ctx.enter_context(nc.sbuf_tensor(name, shape, dt))

        def sem(name):
            return ctx.enter_context(nc.semaphore(name))

        k_halves = sb("k_halves", [128, K_COLS], F32R)
        stage = sb("stage", [128, STAGE_SLOTS, SUBS, 2 * DIM])
        e_t = sb("e_t", [128, PHASES, N])
        split = sb("split", [128, 2, 2, N], F32R)
        moving = sb("moving", [128, MOVING_SLOTS, 2, 2, N], F32R)
        prod = sb("prod", [128, PROD_SLOTS, 4, N])
        k_raw = sb("k_raw", [128, K_SLOTS, PIECE])
        w1_sb = k_raw[:, 0:2, :].rearrange("p a (b n) -> p (a b) n", n=H1)
        w2_sb = k_raw[:, 2, :].rearrange("p (b n) -> p b n", n=H2)
        z_sb = sb("z_sb", [128, Z_BLOCKS, N])
        h1_sb = sb("h1_sb", [128, H1_BLOCKS, N])
        y_sb = h1_sb[0:1, 0, :]
        h2_sb = sb("h2_sb", [128, H2_BLOCKS, N])
        w3_sb = sb("w3_sb", [128, H2_BLOCKS])
        b1_sb = sb("b1_sb", [128, H1_BLOCKS])
        b2_sb = sb("b2_sb", [128, H2_BLOCKS])
        sel = sb("sel", [128, 62])
        ident = sb("ident", [128, 128])
        idx = sb("idx", [128, 2, 32], I32)

        t_ps = ctx.enter_context(nc.psum_tensor("t_ps", [128, T_SLOTS, 4, N], F32))
        z_ps = ctx.enter_context(nc.psum_tensor("z_ps", [128, 2, 512], F32))
        e_ps = ctx.enter_context(nc.psum_tensor("e_ps", [128, 512], F32))
        mlp_ps = ctx.enter_context(nc.psum_tensor("mlp_ps", [128, 512], F32))

        consts_loaded = sem("consts_loaded")
        mlp_weights_loaded = sem("mlp_weights_loaded")
        k_loaded = [sem(f"k_loaded{s}") for s in range(K_SLOTS)]
        k_rounded = sem("k_rounded")
        k_prepared = sem("k_prepared")
        idx_loaded = [sem(f"idx_loaded{h}") for h in range(2)]
        gathered = [sem(f"gathered{s}") for s in range(STAGE_SLOTS)]
        transposed = sem("transposed")
        upper_ready = sem("upper_ready")
        split_ready = sem("split_ready")
        moving_ready = [sem(f"moving_ready{s}") for s in range(MOVING_SLOTS)]
        dense_loaded = [sem(f"dense_loaded{s}") for s in range(2)]
        half_formed = sem("half_formed")
        half_multiplied = sem("half_multiplied")
        item_summed = sem("item_summed")
        z_stored = sem("z_stored")
        mlp_formed = sem("mlp_formed")
        mlp_stored = sem("mlp_stored")
        y_written = sem("y_written")
        slots_granted = sem("slots_granted")
        pairs_seen = sem("pairs_seen")

        def all_tiles(engine, tile):
            tile(0, True, False)
            with engine.Fori(1, TILES - 1) as t:
                tile(t, False, False)
            tile(TILES - 1, False, True)

        block = ctx.enter_context(nc.Block())

        @block.gpsimd
        def _(pool):
            half_pairs = PHASES // 2

            def load_idx(t, half):
                for s in range(STAGE_SLOTS):
                    wait_count(pool, gathered[s], (t * 2 + half - 1) * 64)
                pool.dma_start(idx[:, half, :], ids[t, half]).then_inc(idx_loaded[half], 16)

            def tile(t, first, last):
                for p in range(PHASES):
                    half = p // half_pairs
                    if p % half_pairs == 0:
                        pool.wait_ge(idx_loaded[half], (t + 1) * 16)
                    wait_count(pool, transposed, t * PHASES + p - STAGE_SLOTS + 1)
                    pool.sem_inc(slots_granted, 1)
                    for field in range(2):
                        for sub in range(SUBS):
                            column = (p % half_pairs) * 4 + 2 * field + sub
                            pool.indirect_dma_start(
                                stage[:, p % STAGE_SLOTS, sub, field * DIM:(field + 1) * DIM], None,
                                tables[2 * p + field],
                                bass.IndirectOffsetOnAxis(
                                    ap=idx[:, half, column:column + 1].bitcast(U32), axis=0),
                            ).then_inc(gathered[p % STAGE_SLOTS], 16)
                    if p == half_pairs - 1:
                        load_idx(t, 1)
                    if p == PHASES - 1 and not last:
                        load_idx(t + 1, 0)

            load_idx(0, 0)
            all_tiles(pool, tile)

        @block.sync
        def _(sp):
            def load_k(piece):
                if piece >= K_SLOTS:
                    sp.wait_ge(k_prepared, piece - K_SLOTS + 1)
                for half in range(2):
                    sp.dma_start(k_raw[64 * half:64 * half + 64, piece % K_SLOTS, :],
                                 kernel[:, piece * PIECE:(piece + 1) * PIECE]
                                 ).then_inc(k_loaded[piece % K_SLOTS], 16)

            def spread(t, p):
                pairs_split = t * PHASES + p + 1
                before = t if p >= MOVING_SLOTS else t - 1
                halves_formed = 2 * (before * ITEMS + LAST_ITEM[p - MOVING_SLOTS] + 1)
                sp.wait_ge(split_ready, pairs_split)
                sp.sem_inc(pairs_seen, 1)
                wait_count(sp, half_formed, halves_formed)
                for field in range(2):
                    for half in range(2):
                        sp.dma_start(
                            moving[64 * half:64 * half + 64, p % MOVING_SLOTS, field].bitcast(F32),
                            split[64 * field:64 * field + 64, p % 2].bitcast(F32),
                        ).then_inc(moving_ready[p % MOVING_SLOTS], 16)

            def tile(t, first, last):
                for i in range(ITEMS + 1):
                    if first and i < ITEMS:
                        for piece in K_AT[i]:
                            if piece + K_SLOTS < PIECES:
                                load_k(piece + K_SLOTS)
                            elif piece == PIECES - 1:
                                sp.wait_ge(k_prepared, PIECES)
                                sp.dma_start(w1_sb, w1).then_inc(mlp_weights_loaded, 16)
                                sp.dma_start(w2_sb, w2).then_inc(mlp_weights_loaded, 16)
                    for ahead, p in PREPARE[i]:
                        if not (last and ahead):
                            spread(t + ahead, p)

            for piece in range(K_SLOTS):
                load_k(piece)
            for p in range(EARLY):
                for piece in range(p * K_FIRST // EARLY, (p + 1) * K_FIRST // EARLY):
                    load_k(piece + K_SLOTS)
                spread(0, p)
            all_tiles(sp, tile)

        @block.tensor
        def _(pe):
            def transpose_pair(t, p):
                g = t * PHASES + p
                uses = 2 * t + p // STAGE_SLOTS + 1
                pe.wait_ge(gathered[p % STAGE_SLOTS], uses * 64)
                wait_count(pe, upper_ready, g)
                for sub in range(SUBS):
                    last = nc.tensor.transpose(e_ps[:, sub * 128:(sub + 1) * 128],
                                               stage[:, p % STAGE_SLOTS, sub, :], ident[:])
                last.then_inc(transposed, 1)

            def form(t, i, first):
                item = ITEM_LIST[i]
                if first:
                    pe.wait_ge(k_prepared, last_piece(i) + 1)
                for m in sorted({c // 2 for _, _, c in item["chunks"]}):
                    pe.wait_ge(moving_ready[m % MOVING_SLOTS],
                               (t * (PHASES // MOVING_SLOTS) + m // MOVING_SLOTS + 1) * 64)
                for q, (col, width, c) in enumerate(item["chunks"]):
                    if q % 2 == 0:
                        wait_count(pe, half_multiplied, 2 * (t * ITEMS + i - T_SLOTS) + q // 2 + 1)
                    for half in range(2):
                        last = nc.tensor.matmul(
                            t_ps[0:width, i % T_SLOTS, q, :], k_halves[:, col:col + width],
                            moving[:, (c // 2) % MOVING_SLOTS, c % 2, half, :],
                            start=(half == 0), stop=(half == 1))
                    if q % 2:
                        last.then_inc(half_formed, 1)

            def sum_item(t, i):
                item = ITEM_LIST[i]
                blk, s = divmod(i, ITEMS_PER_BLOCK)
                pe.wait_ge(half_multiplied, 2 * (t * ITEMS + i + 1))
                if item["tail"] is not None:
                    tail = item["tail"]
                    pe.wait_ge(dense_loaded[tail % 2], (t * (len(TAIL_ITEM) // 2) + tail // 2 + 1) * 16)
                if s == 0:
                    wait_count(pe, z_stored, t * Z_BLOCKS + blk - 1)
                for q, (_, width, _) in enumerate(item["chunks"]):
                    rows = 128 if width == 2 * DIM else DIM + 1
                    last = nc.tensor.matmul(
                        z_ps[32 * q:32 * q + 32, blk % 2, 0:N], sel[0:rows, 30 - 2 * s:62 - 2 * s],
                        prod[0:rows, i % PROD_SLOTS, q, :],
                        start=(s == 0), stop=(s == ITEMS_PER_BLOCK - 1))
                last.then_inc(item_summed, 1)

            def sum_two(t, i, first):
                if i >= 0:
                    sum_item(t, i)
                    sum_item(t, i + 1)
                elif not first:
                    sum_item(t - 1, ITEMS + i)
                    sum_item(t - 1, ITEMS + i + 1)

            def mlp_step(t, n):
                if n == 0:
                    pe.wait_ge(mlp_weights_loaded, 32)
                    pe.wait_ge(z_stored, (t + 1) * Z_BLOCKS)
                else:
                    pe.wait_ge(mlp_stored, t * MLP_STEPS + n)
                if n < H1_BLOCKS:
                    out, source, blocks = mlp_ps[:, 0:N], z_sb, Z_BLOCKS
                    weights = w1_sb[:, :, n * 128:(n + 1) * 128]
                elif n < MLP_STEPS - 1:
                    j = n - H1_BLOCKS
                    out, source, blocks = mlp_ps[:, 0:N], h1_sb, H1_BLOCKS
                    weights = w2_sb[:, :, j * 128:(j + 1) * 128]
                else:
                    out, source, blocks = mlp_ps[0:1, 0:N], h2_sb, H2_BLOCKS
                    weights = w3_sb[:].unsqueeze(2)
                for b in range(blocks):
                    last = nc.tensor.matmul(out, weights[:, b, :], source[:, b, :], start=(b == 0),
                                            stop=(b == blocks - 1))
                last.then_inc(mlp_formed, 1)

            def tile(t, first, last):
                for i in range(ITEMS + 1):
                    for ahead, p in PREPARE[i]:
                        if not (last and ahead):
                            transpose_pair(t + ahead, p)
                    if i < ITEMS:
                        form(t, i, first)
                        if i == 0:
                            sum_two(t, -2, first)
                        elif i % 2 and i > 1:
                            sum_two(t, i - SUM_LAG, first)
                        if i in MLP_AT and not first:
                            mlp_step(t - 1, MLP_AT[i])

            pe.wait_ge(consts_loaded, 5 * 16)
            for p in range(EARLY):
                transpose_pair(0, p)
            all_tiles(pe, tile)
            sum_two(TILES, -2, False)
            for n in range(MLP_STEPS):
                mlp_step(TILES - 1, n)

        @block.vector
        def _(dve):
            def k_lower(piece):
                dve.wait_ge(k_rounded, piece + 1)
                cols = slice(piece * PIECE, (piece + 1) * PIECE)
                nc.vector.tensor_tensor(k_halves[64:128, cols], k_raw[64:128, piece % K_SLOTS, :],
                                        k_halves[64:128, cols], ALU.subtract).then_inc(k_prepared, 1)

            def e_lower(t, p):
                dve.wait_ge(upper_ready, t * PHASES + p + 1)
                nc.vector.tensor_tensor(split[:, p % 2, 1, :], e_t[:, p, :], split[:, p % 2, 0, :],
                                        ALU.subtract).then_inc(split_ready, 1)

            def multiply(t, i):
                item = ITEM_LIST[i]
                k, slot, target = item["k"], i % T_SLOTS, prod[:, i % PROD_SLOTS]
                wait_count(dve, item_summed, t * ITEMS + i - PROD_SLOTS + 1)
                for h in range(2):
                    dve.wait_ge(half_formed, 2 * (t * ITEMS + i) + h + 1)
                    if h == 0 or item["tail"] is None:
                        nc.vector.tensor_tensor(
                            target[:, 2 * h:2 * h + 2, :], t_ps[:, slot, 2 * h:2 * h + 2, :],
                            e_t[:, k + h:k + h + 1, :].to_broadcast([128, 2, N]), ALU.mult
                        ).then_inc(half_multiplied, 1)
                    else:
                        nc.vector.tensor_tensor(
                            target[0:DIM, 2:4, :], t_ps[0:DIM, slot, 2:4, :], e_t[0:DIM, k:k + 2, :],
                            ALU.mult).then_inc(half_multiplied, 1)

            def tile(t, first, last):
                for i in range(ITEMS + 1):
                    if i < ITEMS:
                        if first:
                            for piece in K_AT[i]:
                                k_lower(piece)
                        multiply(t, i)
                    for ahead, p in PREPARE[i]:
                        if not (last and ahead):
                            e_lower(t + ahead, p)

            for p in range(EARLY):
                for piece in range(p * K_FIRST // EARLY, (p + 1) * K_FIRST // EARLY):
                    k_lower(piece)
                e_lower(0, p)
            all_tiles(dve, tile)

        @block.scalar
        def _(act):
            def k_upper(piece):
                act.wait_ge(k_loaded[piece % K_SLOTS], (piece // K_SLOTS + 1) * 32)
                nc.scalar.copy(k_halves[:, piece * PIECE:(piece + 1) * PIECE],
                               k_raw[:, piece % K_SLOTS, :]).then_inc(k_rounded, 1)

            def e_upper(t, p):
                g = t * PHASES + p
                act.wait_ge(transposed, g + 1)
                if not isinstance(t, int) or t > 0:
                    act.wait_ge(half_multiplied, 2 * ((t - 1) * ITEMS + LAST_USE[p] + 1))
                nc.scalar.copy(e_t[:, p, :], e_ps[:, 0:N])
                if p >= 2 or not isinstance(t, int) or t > 0:
                    act.wait_ge(moving_ready[(p - 2) % MOVING_SLOTS],
                                (t * (PHASES // MOVING_SLOTS) + (p - 2) // MOVING_SLOTS + 1) * 64)
                nc.scalar.copy(split[:, p % 2, 0, :], e_ps[:, 0:N]).then_inc(upper_ready, 1)

            def load_dense(t, tail):
                i = TAIL_ITEM[tail]
                wait_count(act, item_summed, t * ITEMS + i - PROD_SLOTS + 1)
                act.dma_start(prod[DIM:DIM + 1, i % PROD_SLOTS, 2:4, :], dense[t, tail]
                       ).then_inc(dense_loaded[tail % 2], 16)

            def store_z(t, blk):
                act.wait_ge(item_summed, t * ITEMS + (blk + 1) * ITEMS_PER_BLOCK)
                nc.scalar.copy(z_sb[:, blk, :], z_ps[:, blk % 2, 0:N]).then_inc(z_stored, 1)

            def mlp_step(t, n):
                act.wait_ge(mlp_formed, t * MLP_STEPS + n + 1)
                if n < H1_BLOCKS:
                    nc.scalar.activation(h1_sb[:, n, :], mlp_ps[:, 0:N], ACT.Relu,
                                         bias=b1_sb[:, n:n + 1]).then_inc(mlp_stored, 1)
                elif n < MLP_STEPS - 1:
                    j = n - H1_BLOCKS
                    nc.scalar.activation(h2_sb[:, j, :], mlp_ps[:, 0:N], ACT.Relu,
                                         bias=b2_sb[:, j:j + 1]).then_inc(mlp_stored, 1)
                else:
                    nc.scalar.copy(y_sb, mlp_ps[0:1, 0:N]).then_inc(mlp_stored, 1)
                    act.wait_ge(mlp_stored, (t + 1) * MLP_STEPS)
                    act.dma_start(y_out[t], y_sb).then_inc(y_written, 16)

            def tile(t, first, last):
                for i in range(ITEMS + 1):
                    if first and i < ITEMS:
                        for piece in K_AT[i]:
                            k_upper(piece)
                    for ahead, p in PREPARE[i]:
                        if not (last and ahead):
                            e_upper(t + ahead, p)
                    blk, s = divmod(i - SUM_LAG + 1, ITEMS_PER_BLOCK)
                    if s == 0 and blk > 0:
                        store_z(t, blk - 1)
                    if i == 0 and not first:
                        store_z(t - 1, Z_BLOCKS - 1)
                    if i + 1 in TAIL_ITEM:
                        load_dense(t, TAIL_ITEM.index(i + 1))
                    if i == ITEMS and not last:
                        load_dense(t + 1, 0)
                    if i in MLP_AT and not first:
                        mlp_step(t - 1, MLP_AT[i])
                if not first:
                    act.wait_ge(y_written, t * 16)

            act.dma_start(ident[:], ident_in).then_inc(consts_loaded, 16)
            act.dma_start(sel[:], sel_in).then_inc(consts_loaded, 16)
            act.dma_start(w3_sb[:], w3).then_inc(consts_loaded, 16)
            act.dma_start(b1_sb[:], b1).then_inc(consts_loaded, 16)
            act.dma_start(b2_sb[:], b2).then_inc(consts_loaded, 16)
            load_dense(0, 0)
            act.wait_ge(consts_loaded, 5 * 16)
            for p in range(EARLY):
                for piece in range(p * K_FIRST // EARLY, (p + 1) * K_FIRST // EARLY):
                    k_upper(piece)
                e_upper(0, p)
            all_tiles(act, tile)
            store_z(TILES - 1, Z_BLOCKS - 1)
            for n in range(MLP_STEPS):
                mlp_step(TILES - 1, n)
            act.wait_ge(y_written, TILES * 16)


def kernel(**inputs):
    import concourse.bacc as bacc
    from concourse.bass_utils import run_bass_kernel_spmd

    nc = bacc.Bacc("TRN2", target_bir_lowering=False, num_devices=1)
    arrays = {}

    def give(name, array):
        array = np.ascontiguousarray(array)
        arrays[name] = array
        return nc.dram_tensor(name, array.shape, mybir.dt.from_np(array.dtype),
                              kind="ExternalInput").ap()

    ids = np.asarray(inputs["ids"]).reshape(TILES, SUBS, 128, 2, PHASES // 2, 2)
    ids = give("ids_in", ids.transpose(0, 3, 2, 4, 5, 1).reshape(TILES, 2, 128, 32))
    tables = [give(f"table_{f}", inputs[f"tbl_{f}"]) for f in range(FIELDS)]
    k = give("kernel_in", np.asarray(inputs["L0_rec_kernel"])[:, K_ORDER, :].reshape(DIM, K_COLS))
    w1 = give("w1_in", np.asarray(inputs["W_top1"])[Z_ROWS].reshape(Z_BLOCKS, 128, H1).transpose(1, 0, 2))
    b1 = give("b1_in", np.asarray(inputs["b_top1"]).reshape(H1_BLOCKS, 128).T)
    w2 = give("w2_in", np.asarray(inputs["W_top2"]).reshape(H1_BLOCKS, 128, H2).transpose(1, 0, 2))
    b2 = give("b2_in", np.asarray(inputs["b_top2"]).reshape(H2_BLOCKS, 128).T)
    w3 = give("w3_in", np.asarray(inputs["W_top3"]).reshape(H2_BLOCKS, 128).T)
    dense = np.asarray(inputs["dense_ctx"]).reshape(TILES, N, DENSE // 2, 2)
    dense = give("dense_in", dense.transpose(0, 2, 3, 1).reshape(TILES, DENSE // 2, 1, 2, N))
    sel = np.zeros((128, 62), np.float32)
    sel[0:64, 30] = 1.0
    sel[64:128, 31] = 1.0
    sel = give("sel_in", sel)
    ident = give("ident_in", np.eye(128, dtype=np.float32))
    y = nc.dram_tensor("y_out", (TILES, 1, N), F32, kind="ExternalOutput").ap()
    dlrm_tower(nc, ids, tables, k, w1, b1, w2, b2, w3, dense, sel, ident, y)
    result = run_bass_kernel_spmd(nc, [arrays], core_ids=[0])
    return result.results[0]["y_out"].reshape(BATCH, 1)
```

```python
from contextlib import ExitStack

import numpy as np

import concourse.bass as bass
from concourse import mybir

F32 = mybir.dt.float32
F32R = mybir.dt.float32r
I32 = mybir.dt.int32
U32 = mybir.dt.uint32
ALU = mybir.AluOpType
ACT = mybir.ActivationFunctionType

BATCH, FIELDS, DIM, DENSE = 2048, 32, 64, 16
H1, H2 = 512, 256
PAIRS = FIELDS * (FIELDS - 1) // 2
PHASES = FIELDS // 2
N = 256
SUBS = N // 128
TILES = BATCH // N
K_COLS = PAIRS * DIM
PIECE = 1024
PIECES = K_COLS // PIECE
K_LOADS = (PIECES + 1) // 2
Z_BLOCKS = (PAIRS + DENSE) // 128
H1_BLOCKS, H2_BLOCKS = H1 // 128, H2 // 128
MLP_STEPS = H1_BLOCKS + H2_BLOCKS + 1
MLP_AT = {n + 1: n for n in range(MLP_STEPS)}

STAGE_SLOTS = 8
MOVING_SLOTS = 4
T_SLOTS = 2
PROD_SLOTS = 4
SUM_LAG = 3
K_SLOTS = 5


def plan():
    k_order, at = [], {}
    for m in range(PHASES):
        at[(2 * m, 2 * m + 1)] = len(k_order) * DIM
        k_order.append((2 * m, 2 * m + 1))
        for k in ([m - 1] if m % 2 else []) + list(range(m - m % 2)):
            for c in (2 * m, 2 * m + 1):
                for r in (2 * k, 2 * k + 1):
                    at[(r, c)] = len(k_order) * DIM
                    k_order.append((r, c))

    items = []
    for m in range(PHASES):
        if m % 2:
            chunks = [(at[(2 * m - 2, c)], 2 * DIM, c) for c in (2 * m, 2 * m + 1)]
            chunks += [(at[(2 * n, 2 * n + 1)], DIM, 2 * n + 1) for n in (m - 1, m)]
            items.append({"m": m, "k": m - 1, "tail": m // 2, "chunks": chunks})
        for k in range(0, m - 1, 2):
            chunks = [(at[(2 * kk, c)], 2 * DIM, c) for kk in (k, k + 1) for c in (2 * m, 2 * m + 1)]
            items.append({"m": m, "k": k, "tail": None, "chunks": chunks})

    def pair_row(r, c):
        return r * (FIELDS - 1) - r * (r - 1) // 2 + c - r - 1

    z_rows = [None] * (PAIRS + DENSE)
    per_block = len(items) // Z_BLOCKS
    for i, item in enumerate(items):
        for q, (_, columns, c) in enumerate(item["chunks"]):
            row = 128 * (i // per_block) + 32 * q + 2 * (i % per_block)
            if columns == DIM:
                z_rows[row] = pair_row(c - 1, c)
                z_rows[row + 1] = PAIRS + 2 * item["tail"] + q - 2
            else:
                k = item["k"] + (q // 2 if item["tail"] is None else 0)
                z_rows[row] = pair_row(2 * k, c)
                z_rows[row + 1] = pair_row(2 * k + 1, c)
    assert sorted(z_rows) == list(range(PAIRS + DENSE))
    return [pair_row(r, c) for r, c in k_order], items, z_rows


HALVES = (slice(0, 64), slice(64, 128))
K_ORDER, ITEM_LIST, Z_ROWS = plan()
ITEMS = len(ITEM_LIST)
ITEMS_PER_BLOCK = ITEMS // Z_BLOCKS
FIRST_ITEM = [next(i for i, x in enumerate(ITEM_LIST) if x["m"] >= m) for m in range(PHASES)]
LAST_ITEM = [max(i for i, x in enumerate(ITEM_LIST) if m in {c // 2 for _, _, c in x["chunks"]})
             for m in range(PHASES)]
LAST_USE = [max(i for i, x in enumerate(ITEM_LIST) if k in (x["k"], x["k"] + 1))
            for k in range(PHASES)]
TAIL_ITEM = [i for i, x in enumerate(ITEM_LIST) if x["tail"] is not None]

EARLY = 4
PREPARE = {i: [] for i in range(ITEMS + 1)}
for _p in range(EARLY, PHASES):
    PREPARE[max(LAST_ITEM[_p - MOVING_SLOTS] + 1, FIRST_ITEM[_p] - 6, _p - 3)].append((0, _p))
for _p in range(EARLY - 1):
    PREPARE[FIRST_ITEM[PHASES - 1] + 2 + 2 * _p].append((1, _p))
PREPARE[ITEMS].append((1, EARLY - 1))
FIRST_EARLY = 2
PREPARE_FIRST = {i: [] for i in range(ITEMS + 1)}
for _p in range(FIRST_EARLY, PHASES):
    PREPARE_FIRST[max(LAST_ITEM[_p - MOVING_SLOTS] + 1 if _p >= MOVING_SLOTS else 0,
                      FIRST_ITEM[_p] - min(6, _p // 2))].append((0, _p))
for _i in PREPARE:
    PREPARE_FIRST[_i] += [x for x in PREPARE[_i] if x[0]]


def last_piece(i):
    return max(col + width - 1 for col, width, _ in ITEM_LIST[i]["chunks"]) // PIECE


K_LEAD = 14
K_AHEAD = 3
K_EARLY = {-2: 5, -1: 3, 0: 1, FIRST_ITEM[2]: 2, FIRST_ITEM[3]: 2, FIRST_ITEM[4]: 1,
           FIRST_ITEM[5]: 1, FIRST_ITEM[6]: 1, FIRST_ITEM[7]: 1}
K_LOWER_AT = {i: [] for i in range(-2, ITEMS)}
_place = [i for i, n in K_EARLY.items() for _ in range(n)]
for _piece in range(len(_place), PIECES):
    _first = next(i for i in range(ITEMS) if last_piece(i) >= _piece)
    _place.append(max(_place[-1], _first - K_LEAD))
K_UPPER_AT = {i: [] for i in range(-2, ITEMS)}
for _piece in range(PIECES):
    K_LOWER_AT[_place[_piece]].append(_piece)
    K_UPPER_AT[_place[max(0, _piece - K_AHEAD)]].append(_piece)
K_POOL_AT = {7 + n: [piece] for n, piece in enumerate(range(12, PIECES - 3, 2))}
K_POOL_AT[PHASES - 1] = [PIECES - 3, PIECES - 1]
POOL_PIECES = [piece for pieces in K_POOL_AT.values() for piece in pieces]
assert not any(piece % 2 for piece in POOL_PIECES)


def pool_prepares(last):
    return sum(piece <= last for piece in POOL_PIECES)


def wait_count(engine, semaphore, count):
    if isinstance(count, int) and count <= 0:
        return
    engine.wait_ge(semaphore, count)


def dlrm_tower(nc, ids, tables, kernel, w1, b1, w2, b2, w3, dense, sel_in, ident_in, y_out):
    ctx = ExitStack()
    with ctx:
        def sb(name, shape, dt=F32):
            return ctx.enter_context(nc.sbuf_tensor(name, shape, dt))

        def sem(name):
            return ctx.enter_context(nc.semaphore(name))

        k_halves = sb("k_halves", [128, K_COLS], F32R)
        stage = sb("stage", [128, STAGE_SLOTS, SUBS, 2 * DIM])
        e_t = sb("e_t", [128, PHASES, N])
        moving = sb("moving", [128, MOVING_SLOTS, 2, 2, N], F32R)
        prod = sb("prod", [128, PROD_SLOTS, 4, N])
        k_raw = sb("k_raw", [128, K_SLOTS - 1, PIECE])
        w1_sb = k_raw[:, 0:2, :].rearrange("p a (b n) -> p (a b) n", n=H1)
        w2_sb = k_raw[:, 2].rearrange("p (b n) -> p b n", n=H2)
        z_sb = sb("z_sb", [128, Z_BLOCKS, N])
        h1_sb = sb("h1_sb", [128, H1_BLOCKS, N])
        k_slot = [k_raw[:, s, :] for s in range(K_SLOTS - 1)] + [h1_sb[:].rearrange("p b n -> p (b n)")]
        y_sb = h1_sb[0:1, 0, :]
        h2_sb = sb("h2_sb", [128, H2_BLOCKS, N])
        w3_sb = sb("w3_sb", [128, H2_BLOCKS])
        b1_sb = sb("b1_sb", [128, H1_BLOCKS])
        b2_sb = sb("b2_sb", [128, H2_BLOCKS])
        sel = sb("sel", [128, 62])
        ident = sb("ident", [128, 128])
        idx = sb("idx", [128, 2, 32], I32)

        t_ps = ctx.enter_context(nc.psum_tensor("t_ps", [128, T_SLOTS, 4, N], F32))
        z_ps = ctx.enter_context(nc.psum_tensor("z_ps", [128, 2, 512], F32))
        e_ps = ctx.enter_context(nc.psum_tensor("e_ps", [128, 512], F32))
        mlp_ps = ctx.enter_context(nc.psum_tensor("mlp_ps", [128, 512], F32))

        ident_loaded = sem("ident_loaded")
        sel_loaded = sem("sel_loaded")
        mlp_weights_loaded = sem("mlp_weights_loaded")
        k_loaded = [sem(f"k_loaded{s}") for s in range(K_SLOTS)]
        k_rounded = sem("k_rounded")
        k_prepared = sem("k_prepared")
        k_prepared_pool = sem("k_prepared_pool")
        idx_loaded = [sem(f"idx_loaded{h}") for h in range(2)]
        first_idx_loaded = sem("first_idx_loaded")
        gathered = [sem(f"gathered{s}") for s in range(STAGE_SLOTS)]
        transposed = sem("transposed")
        upper_ready = sem("upper_ready")
        lower_ready = sem("lower_ready")
        moving_ready = sem("moving_ready")
        dense_loaded = [sem(f"dense_loaded{s}") for s in range(2)]
        half_formed = sem("half_formed")
        half_multiplied = sem("half_multiplied")
        item_summed = sem("item_summed")
        z_stored = sem("z_stored")
        mlp_formed = sem("mlp_formed")
        mlp_stored = sem("mlp_stored")
        y_written = sem("y_written")
        slots_granted = sem("slots_granted")

        def all_tiles(engine, tile):
            tile(0, True, False)
            with engine.Fori(1, TILES - 1) as t:
                tile(t, False, False)
            tile(TILES - 1, False, True)

        def wait_for_k(engine, piece):
            engine.wait_ge(k_prepared, piece + 1 - pool_prepares(piece))
            wait_count(engine, k_prepared_pool, pool_prepares(piece))

        def k_lower(tensor_tensor, prepared, piece):
            here, there = HALVES[piece % 2], HALVES[1 - piece % 2]
            cols = slice(piece * PIECE, (piece + 1) * PIECE)
            tensor_tensor(k_halves[there, cols], k_slot[piece // 2 % K_SLOTS][here],
                          k_halves[here, cols], ALU.subtract).then_inc(prepared, 1)

        block = ctx.enter_context(nc.Block())

        @block.gpsimd
        def _(pool):
            half_pairs = PHASES // 2

            def load_idx(t, half):
                for s in range(STAGE_SLOTS):
                    wait_count(pool, gathered[s], (t * 2 + half - 1) * 64)
                pool.dma_start(idx[:, half, :], ids[t, half]).then_inc(idx_loaded[half], 16)

            def tile(t, first, last):
                for p in range(PHASES):
                    half = p // half_pairs
                    if p % half_pairs == 0:
                        if first and half == 0:
                            pool.wait_ge(first_idx_loaded, 16)
                        else:
                            pool.wait_ge(idx_loaded[half], (t + half) * 16)
                    wait_count(pool, transposed, t * PHASES + p - STAGE_SLOTS + 1)
                    pool.sem_inc(slots_granted, 1)
                    for field in range(2):
                        for sub in range(SUBS):
                            column = (p % half_pairs) * 4 + 2 * field + sub
                            pool.indirect_dma_start(
                                stage[:, p % STAGE_SLOTS, sub, field * DIM:(field + 1) * DIM], None,
                                tables[2 * p + field],
                                bass.IndirectOffsetOnAxis(
                                    ap=idx[:, half, column:column + 1].bitcast(U32), axis=0),
                            ).then_inc(gathered[p % STAGE_SLOTS], 16)
                    if p == half_pairs - 1:
                        load_idx(t, 1)
                    if first:
                        for piece in K_POOL_AT.get(p, []):
                            pool.wait_ge(k_rounded, piece + 1)
                            k_lower(nc.gpsimd.tensor_tensor, k_prepared_pool, piece)
                    if p == PHASES - 1 and not last:
                        load_idx(t + 1, 0)

            all_tiles(pool, tile)

        @block.sync
        def _(sp):
            def load_k(load):
                if load >= K_SLOTS:
                    wait_for_k(sp, 2 * (load - K_SLOTS) + 1)
                partitions = 128 if 2 * load + 1 < PIECES else 64
                sp.dma_start(k_slot[load % K_SLOTS][0:partitions], kernel[load, 0:partitions]
                             ).then_inc(k_loaded[load % K_SLOTS], 16)

            def after_piece(piece):
                if piece % 2 and piece // 2 + K_SLOTS < K_LOADS:
                    load_k(piece // 2 + K_SLOTS)
                if piece == PIECES - 1:
                    wait_for_k(sp, piece)
                    for to, source in ((w1_sb, w1), (w2_sb, w2), (w3_sb[:], w3), (b1_sb[:], b1),
                                       (b2_sb[:], b2)):
                        sp.dma_start(to, source).then_inc(mlp_weights_loaded, 16)

            def load_dense(t, tail):
                i = TAIL_ITEM[tail]
                wait_count(sp, item_summed, t * ITEMS + i - PROD_SLOTS + 1)
                sp.dma_start(prod[DIM:DIM + 1, i % PROD_SLOTS, 2:4, :], dense[t, tail]
                             ).then_inc(dense_loaded[tail % 2], 16)

            def tile(t, first, last):
                for i in range(ITEMS):
                    if first:
                        for piece in K_LOWER_AT[i]:
                            after_piece(piece)
                    if i + 1 in TAIL_ITEM:
                        load_dense(t, TAIL_ITEM.index(i + 1))
                if not last:
                    load_dense(t + 1, 0)

            sp.dma_start(ident[:], ident_in).then_inc(ident_loaded, 16)
            load_k(0)
            load_k(1)
            sp.dma_start(sel[:], sel_in).then_inc(sel_loaded, 16)
            for load in range(2, K_SLOTS):
                load_k(load)
            load_dense(0, 0)
            for piece in K_LOWER_AT[-2] + K_LOWER_AT[-1]:
                after_piece(piece)
            all_tiles(sp, tile)

        @block.tensor
        def _(pe):
            def transpose_pair(t, p):
                g = t * PHASES + p
                uses = 2 * t + p // STAGE_SLOTS + 1
                pe.wait_ge(gathered[p % STAGE_SLOTS], uses * 64)
                wait_count(pe, upper_ready, g)
                for sub in range(SUBS):
                    last = nc.tensor.transpose(e_ps[:, sub * 128:(sub + 1) * 128],
                                               stage[:, p % STAGE_SLOTS, sub, :], ident[:])
                last.then_inc(transposed, 1)

            def form(t, i, first):
                item = ITEM_LIST[i]
                if first:
                    wait_for_k(pe, last_piece(i))
                pe.wait_ge(moving_ready, t * PHASES + item["m"] + 1)
                for q, (col, width, c) in enumerate(item["chunks"]):
                    if q % 2 == 0:
                        wait_count(pe, half_multiplied, 2 * (t * ITEMS + i - T_SLOTS) + q // 2 + 1)
                    for half in range(2):
                        last = nc.tensor.matmul(
                            t_ps[0:width, i % T_SLOTS, q, :], k_halves[:, col:col + width],
                            moving[:, (c // 2) % MOVING_SLOTS, c % 2, half, :],
                            start=(half == 0), stop=(half == 1))
                    if q % 2:
                        last.then_inc(half_formed, 1)

            def sum_item(t, i):
                item = ITEM_LIST[i]
                blk, s = divmod(i, ITEMS_PER_BLOCK)
                pe.wait_ge(half_multiplied, 2 * (t * ITEMS + i + 1))
                if item["tail"] is not None:
                    tail = item["tail"]
                    pe.wait_ge(dense_loaded[tail % 2], (t * (len(TAIL_ITEM) // 2) + tail // 2 + 1) * 16)
                if s == 0:
                    wait_count(pe, z_stored, t * Z_BLOCKS + blk - 1)
                for q, (_, width, _) in enumerate(item["chunks"]):
                    rows = 128 if width == 2 * DIM else DIM + 1
                    last = nc.tensor.matmul(
                        z_ps[32 * q:32 * q + 32, blk % 2, 0:N], sel[0:rows, 30 - 2 * s:62 - 2 * s],
                        prod[0:rows, i % PROD_SLOTS, q, :],
                        start=(s == 0), stop=(s == ITEMS_PER_BLOCK - 1))
                last.then_inc(item_summed, 1)

            def sum_two(t, i, first):
                if i >= 0:
                    sum_item(t, i)
                    sum_item(t, i + 1)
                elif not first:
                    sum_item(t - 1, ITEMS + i)
                    sum_item(t - 1, ITEMS + i + 1)

            def mlp_step(t, n, final=False):
                if n == 0:
                    pe.wait_ge(mlp_weights_loaded, 5 * 16)
                    pe.wait_ge(z_stored, (t + 1) * Z_BLOCKS)
                elif final:
                    stored = n if n in (H1_BLOCKS, MLP_STEPS - 1) else n - 1
                    wait_count(pe, mlp_stored, t * MLP_STEPS + stored)
                else:
                    pe.wait_ge(mlp_stored, t * MLP_STEPS + n)
                ps = e_ps if final and n % 2 else mlp_ps
                if n < H1_BLOCKS:
                    out, source, blocks = ps[:, 0:N], z_sb, Z_BLOCKS
                    weights = w1_sb[:, :, n * 128:(n + 1) * 128]
                elif n < MLP_STEPS - 1:
                    j = n - H1_BLOCKS
                    out, source, blocks = ps[:, 0:N], h1_sb, H1_BLOCKS
                    weights = w2_sb[:, :, j * 128:(j + 1) * 128]
                else:
                    out, source, blocks = ps[0:1, 0:N], h2_sb, H2_BLOCKS
                    weights = w3_sb[:].unsqueeze(2)
                for b in range(blocks):
                    last = nc.tensor.matmul(out, weights[:, b, :], source[:, b, :], start=(b == 0),
                                            stop=(b == blocks - 1))
                last.then_inc(mlp_formed, 1)

            def tile(t, first, last):
                for i in range(ITEMS + 1):
                    for ahead, p in (PREPARE_FIRST if first else PREPARE)[i]:
                        if not (last and ahead):
                            transpose_pair(t + ahead, p)
                    if i < ITEMS:
                        form(t, i, first)
                        if i == 0:
                            sum_two(t, -2, first)
                        elif i % 2 and i > 1:
                            sum_two(t, i - SUM_LAG, first)
                        if i in MLP_AT and not first:
                            mlp_step(t - 1, MLP_AT[i])

            pe.wait_ge(ident_loaded, 16)
            for p in range(FIRST_EARLY):
                transpose_pair(0, p)
            pe.wait_ge(sel_loaded, 16)
            all_tiles(pe, tile)
            sum_two(TILES, -2, False)
            pe.wait_ge(upper_ready, TILES * PHASES)
            for n in range(MLP_STEPS):
                mlp_step(TILES - 1, n, final=True)

        @block.vector
        def _(dve):
            def prepare_k(i):
                for piece in K_LOWER_AT[i]:
                    if piece not in POOL_PIECES:
                        dve.wait_ge(k_rounded, piece + 1)
                        k_lower(nc.vector.tensor_tensor, k_prepared, piece)

            def e_lower(t, p):
                dve.wait_ge(upper_ready, t * PHASES + p + 1)
                for field, here in enumerate(HALVES):
                    done = nc.vector.tensor_tensor(
                        moving[here, p % MOVING_SLOTS, field, 1, :], e_t[here, p, :],
                        moving[here, p % MOVING_SLOTS, field, 0, :], ALU.subtract)
                done.then_inc(lower_ready, 1)

            def multiply(t, i):
                item = ITEM_LIST[i]
                k, slot, target = item["k"], i % T_SLOTS, prod[:, i % PROD_SLOTS]
                wait_count(dve, item_summed, t * ITEMS + i - PROD_SLOTS + 1)
                for h in range(2):
                    dve.wait_ge(half_formed, 2 * (t * ITEMS + i) + h + 1)
                    if h == 0 or item["tail"] is None:
                        nc.vector.tensor_tensor(
                            target[:, 2 * h:2 * h + 2, :], t_ps[:, slot, 2 * h:2 * h + 2, :],
                            e_t[:, k + h:k + h + 1, :].to_broadcast([128, 2, N]), ALU.mult
                        ).then_inc(half_multiplied, 1)
                    else:
                        nc.vector.tensor_tensor(
                            target[0:DIM, 2:4, :], t_ps[0:DIM, slot, 2:4, :], e_t[0:DIM, k:k + 2, :],
                            ALU.mult).then_inc(half_multiplied, 1)

            def prepare(t, i, first, last):
                for ahead, p in (PREPARE_FIRST if first else PREPARE)[i]:
                    if not (last and ahead):
                        e_lower(t + ahead, p)

            def tile(t, first, last):
                for i in range(ITEMS):
                    if first:
                        prepare(t, i, first, last)
                        prepare_k(i)
                    multiply(t, i)
                    if not first:
                        prepare(t, i, first, last)
                prepare(t, ITEMS, first, last)

            for p in range(FIRST_EARLY):
                prepare_k(p - FIRST_EARLY)
                e_lower(0, p)
            all_tiles(dve, tile)

        @block.scalar
        def _(act):
            def k_upper(piece):
                load = piece // 2
                act.wait_ge(k_loaded[load % K_SLOTS], (load // K_SLOTS + 1) * 16)
                here = HALVES[piece % 2]
                nc.scalar.copy(k_halves[here, piece * PIECE:(piece + 1) * PIECE],
                               k_slot[load % K_SLOTS][here]).then_inc(k_rounded, 1)

            def e_upper(t, p):
                act.wait_ge(transposed, t * PHASES + p + 1)
                if not isinstance(t, int) or t > 0:
                    act.wait_ge(half_multiplied, 2 * ((t - 1) * ITEMS + LAST_USE[p] + 1))
                nc.scalar.copy(e_t[:, p, :], e_ps[:, 0:N])
                before = t if p >= MOVING_SLOTS else t - 1
                wait_count(act, half_formed, 2 * (before * ITEMS + LAST_ITEM[p - MOVING_SLOTS] + 1))
                for field, here in enumerate(HALVES):
                    done = nc.scalar.copy(moving[here, p % MOVING_SLOTS, field, 0, :],
                                          e_ps[here, 0:N])
                done.then_inc(upper_ready, 1)

            def e_across(t, p):
                act.wait_ge(lower_ready, t * PHASES + p + 1)
                for field, here in enumerate(HALVES):
                    done = nc.scalar.copy(moving[HALVES[1 - field], p % MOVING_SLOTS, field],
                                          moving[here, p % MOVING_SLOTS, field])
                done.then_inc(moving_ready, 1)

            def store_z(t, blk):
                act.wait_ge(item_summed, t * ITEMS + (blk + 1) * ITEMS_PER_BLOCK)
                nc.scalar.copy(z_sb[:, blk, :], z_ps[:, blk % 2, 0:N]).then_inc(z_stored, 1)

            def mlp_step(t, n, final=False):
                act.wait_ge(mlp_formed, t * MLP_STEPS + n + 1)
                ps = e_ps if final and n % 2 else mlp_ps
                if n < H1_BLOCKS:
                    nc.scalar.activation(h1_sb[:, n, :], ps[:, 0:N], ACT.Relu,
                                         bias=b1_sb[:, n:n + 1]).then_inc(mlp_stored, 1)
                elif n < MLP_STEPS - 1:
                    j = n - H1_BLOCKS
                    nc.scalar.activation(h2_sb[:, j, :], ps[:, 0:N], ACT.Relu,
                                         bias=b2_sb[:, j:j + 1]).then_inc(mlp_stored, 1)
                else:
                    nc.scalar.copy(y_sb, ps[0:1, 0:N]).then_inc(mlp_stored, 1)
                    act.wait_ge(mlp_stored, (t + 1) * MLP_STEPS)
                    act.dma_start(y_out[t], y_sb).then_inc(y_written, 16)

            def tile(t, first, last):
                for i in range(ITEMS + 1):
                    for ahead, p in (PREPARE_FIRST if first else PREPARE)[i]:
                        if not (last and ahead):
                            e_upper(t + ahead, p)
                            e_across(t + ahead, p)
                    if first and i < ITEMS:
                        for piece in K_UPPER_AT[i]:
                            k_upper(piece)
                    blk, s = divmod(i - SUM_LAG + 1, ITEMS_PER_BLOCK)
                    if s == 0 and blk > 0:
                        store_z(t, blk - 1)
                    if i == 0 and not first:
                        store_z(t - 1, Z_BLOCKS - 1)
                    if i in MLP_AT and not first:
                        mlp_step(t - 1, MLP_AT[i])
                if not first:
                    act.wait_ge(y_written, t * 16)

            act.dma_start(idx[:, 0, :], ids[0, 0]).then_inc(first_idx_loaded, 16)
            for p in range(FIRST_EARLY):
                for piece in K_UPPER_AT[p - FIRST_EARLY]:
                    k_upper(piece)
                e_upper(0, p)
                e_across(0, p)
            all_tiles(act, tile)
            store_z(TILES - 1, Z_BLOCKS - 1)
            for n in range(MLP_STEPS):
                mlp_step(TILES - 1, n, final=True)
            act.wait_ge(y_written, TILES * 16)


def kernel(**inputs):
    import concourse.bacc as bacc
    from concourse.bass_utils import run_bass_kernel_spmd

    nc = bacc.Bacc("TRN2", target_bir_lowering=False, num_devices=1)
    arrays = {}

    def give(name, array):
        array = np.ascontiguousarray(array)
        arrays[name] = array
        return nc.dram_tensor(name, array.shape, mybir.dt.from_np(array.dtype),
                              kind="ExternalInput").ap()

    ids = np.asarray(inputs["ids"]).reshape(TILES, SUBS, 128, 2, PHASES // 2, 2)
    ids = give("ids_in", ids.transpose(0, 3, 2, 4, 5, 1).reshape(TILES, 2, 128, 32))
    tables = [give(f"table_{f}", inputs[f"tbl_{f}"]) for f in range(FIELDS)]
    k = np.asarray(inputs["L0_rec_kernel"])[:, K_ORDER, :].reshape(DIM, PIECES, PIECE)
    k = np.concatenate([k, k[:, :2 * K_LOADS - PIECES]], axis=1).transpose(1, 0, 2)
    k = give("kernel_in", k.reshape(K_LOADS, 2 * DIM, PIECE))
    w1 = give("w1_in", np.asarray(inputs["W_top1"])[Z_ROWS].reshape(Z_BLOCKS, 128, H1).transpose(1, 0, 2))
    b1 = give("b1_in", np.asarray(inputs["b_top1"]).reshape(H1_BLOCKS, 128).T)
    w2 = give("w2_in", np.asarray(inputs["W_top2"]).reshape(H1_BLOCKS, 128, H2).transpose(1, 0, 2))
    b2 = give("b2_in", np.asarray(inputs["b_top2"]).reshape(H2_BLOCKS, 128).T)
    w3 = give("w3_in", np.asarray(inputs["W_top3"]).reshape(H2_BLOCKS, 128).T)
    dense = np.asarray(inputs["dense_ctx"]).reshape(TILES, N, DENSE // 2, 2)
    dense = give("dense_in", dense.transpose(0, 2, 3, 1).reshape(TILES, DENSE // 2, 1, 2, N))
    sel = np.zeros((128, 62), np.float32)
    sel[0:64, 30] = 1.0
    sel[64:128, 31] = 1.0
    sel = give("sel_in", sel)
    ident = give("ident_in", np.eye(128, dtype=np.float32))
    y = nc.dram_tensor("y_out", (TILES, 1, N), F32, kind="ExternalOutput").ap()
    dlrm_tower(nc, ids, tables, k, w1, b1, w2, b2, w3, dense, sel, ident, y)
    result = run_bass_kernel_spmd(nc, [arrays], core_ids=[0])
    return result.results[0]["y_out"].reshape(BATCH, 1)
```

```python
from contextlib import ExitStack

import numpy as np

import concourse.bass as bass
from concourse import mybir

F32 = mybir.dt.float32
F32R = mybir.dt.float32r
I32 = mybir.dt.int32
U32 = mybir.dt.uint32
ALU = mybir.AluOpType
ACT = mybir.ActivationFunctionType

BATCH, FIELDS, DIM, DENSE = 2048, 32, 64, 16
H1, H2 = 512, 256
PAIRS = FIELDS * (FIELDS - 1) // 2
PHASES = FIELDS // 2
N = 256
SUBS = N // 128
TILES = BATCH // N
K_COLS = PAIRS * DIM
PIECE = 1024
PIECES = K_COLS // PIECE
K_LOADS = (PIECES + 1) // 2
Z_BLOCKS = (PAIRS + DENSE) // 128
H1_BLOCKS, H2_BLOCKS = H1 // 128, H2 // 128
MLP_STEPS = H1_BLOCKS + H2_BLOCKS + 1
MLP_AT = {n + 1: n for n in range(MLP_STEPS)}

STAGE_SLOTS = 8
MOVING_SLOTS = 4
T_SLOTS = 2
PROD_SLOTS = 4
SUM_LAG = 3
K_SLOTS = 5


def plan():
    k_order, at = [], {}
    for m in range(PHASES):
        at[(2 * m, 2 * m + 1)] = len(k_order) * DIM
        k_order.append((2 * m, 2 * m + 1))
        for k in ([m - 1] if m % 2 else []) + list(range(m - m % 2)):
            for c in (2 * m, 2 * m + 1):
                for r in (2 * k, 2 * k + 1):
                    at[(r, c)] = len(k_order) * DIM
                    k_order.append((r, c))

    items = []
    for m in range(PHASES):
        if m % 2:
            chunks = [(at[(2 * m - 2, c)], 2 * DIM, c) for c in (2 * m, 2 * m + 1)]
            chunks += [(at[(2 * n, 2 * n + 1)], DIM, 2 * n + 1) for n in (m - 1, m)]
            items.append({"m": m, "k": m - 1, "tail": m // 2, "chunks": chunks})
        for k in range(0, m - 1, 2):
            chunks = [(at[(2 * kk, c)], 2 * DIM, c) for kk in (k, k + 1) for c in (2 * m, 2 * m + 1)]
            items.append({"m": m, "k": k, "tail": None, "chunks": chunks})

    def pair_row(r, c):
        return r * (FIELDS - 1) - r * (r - 1) // 2 + c - r - 1

    z_rows = [None] * (PAIRS + DENSE)
    per_bank = 2 * len(items) // Z_BLOCKS
    for i, item in enumerate(items):
        bank, s = divmod(i, per_bank)
        for q, (_, columns, c) in enumerate(item["chunks"]):
            row = 128 * (2 * bank + s % 2) + 32 * q + 2 * (s // 2)
            if columns == DIM:
                z_rows[row] = pair_row(c - 1, c)
                z_rows[row + 1] = PAIRS + 2 * item["tail"] + q - 2
            else:
                k = item["k"] + (q // 2 if item["tail"] is None else 0)
                z_rows[row] = pair_row(2 * k, c)
                z_rows[row + 1] = pair_row(2 * k + 1, c)
    assert sorted(z_rows) == list(range(PAIRS + DENSE))
    return [pair_row(r, c) for r, c in k_order], items, z_rows


HALVES = (slice(0, 64), slice(64, 128))
K_ORDER, ITEM_LIST, Z_ROWS = plan()
ITEMS = len(ITEM_LIST)
Z_BANKS = Z_BLOCKS // 2
ITEMS_PER_BANK = ITEMS // Z_BANKS
FIRST_ITEM = [next(i for i, x in enumerate(ITEM_LIST) if x["m"] >= m) for m in range(PHASES)]
LAST_ITEM = [max(i for i, x in enumerate(ITEM_LIST) if m in {c // 2 for _, _, c in x["chunks"]})
             for m in range(PHASES)]
LAST_USE = [max(i for i, x in enumerate(ITEM_LIST) if k in (x["k"], x["k"] + 1))
            for k in range(PHASES)]
TAIL_ITEM = [i for i, x in enumerate(ITEM_LIST) if x["tail"] is not None]

EARLY = 4
PREPARE = {i: [] for i in range(ITEMS + 1)}
for _p in range(EARLY, PHASES):
    PREPARE[max(LAST_ITEM[_p - MOVING_SLOTS] + 1, FIRST_ITEM[_p] - 6, 2 * _p - 7)].append((0, _p))
for _p in range(EARLY - 1):
    PREPARE[FIRST_ITEM[PHASES - 1] + 2 + 2 * _p].append((1, _p))
PREPARE[ITEMS].append((1, EARLY - 1))
FIRST_EARLY = 2
PREPARE_FIRST = {i: [] for i in range(ITEMS + 1)}
for _p in range(FIRST_EARLY, PHASES):
    PREPARE_FIRST[max(LAST_ITEM[_p - MOVING_SLOTS] + 1 if _p >= MOVING_SLOTS else 0,
                      FIRST_ITEM[_p] - min(6, _p // 2))].append((0, _p))
for _i in PREPARE:
    PREPARE_FIRST[_i] += [x for x in PREPARE[_i] if x[0]]


def last_piece(i):
    return max(col + width - 1 for col, width, _ in ITEM_LIST[i]["chunks"]) // PIECE


K_LEAD = 14
K_AHEAD = 3
K_EARLY = {-2: 5, -1: 3, 0: 1, FIRST_ITEM[2]: 2, FIRST_ITEM[3]: 2, FIRST_ITEM[4]: 1,
           FIRST_ITEM[5]: 1, FIRST_ITEM[6]: 1, FIRST_ITEM[7]: 1}
K_LOWER_AT = {i: [] for i in range(-2, ITEMS)}
_place = [i for i, n in K_EARLY.items() for _ in range(n)]
for _piece in range(len(_place), PIECES):
    _first = next(i for i in range(ITEMS) if last_piece(i) >= _piece)
    _place.append(max(_place[-1], _first - K_LEAD))
K_UPPER_AT = {i: [] for i in range(-2, ITEMS)}
for _piece in range(PIECES):
    K_LOWER_AT[_place[_piece]].append(_piece)
    K_UPPER_AT[_place[max(0, _piece - K_AHEAD)]].append(_piece)
K_POOL_AT = {7 + n: [piece] for n, piece in enumerate(range(12, PIECES - 3, 2))}
K_POOL_AT[PHASES - 1] = [PIECES - 3, PIECES - 1]
POOL_PIECES = [piece for pieces in K_POOL_AT.values() for piece in pieces]
assert not any(piece % 2 for piece in POOL_PIECES)


def pool_prepares(last):
    return sum(piece <= last for piece in POOL_PIECES)


def wait_count(engine, semaphore, count):
    if isinstance(count, int) and count <= 0:
        return
    engine.wait_ge(semaphore, count)


def dlrm_tower(nc, ids, tables, kernel, w1, b1, w2, b2, w3, dense, sel_in, ident_in, y_out):
    ctx = ExitStack()
    with ctx:
        def sb(name, shape, dt=F32):
            return ctx.enter_context(nc.sbuf_tensor(name, shape, dt))

        def sem(name):
            return ctx.enter_context(nc.semaphore(name))

        def prod_slot(i):
            return prod[:, i // 2 % (PROD_SLOTS // 2), :, i % 2, :]

        k_halves = sb("k_halves", [128, K_COLS], F32R)
        stage = sb("stage", [128, STAGE_SLOTS, SUBS, 2 * DIM])
        e_t = sb("e_t", [128, PHASES, N])
        moving = sb("moving", [128, MOVING_SLOTS, 2, 2, N], F32R)
        prod = sb("prod", [128, PROD_SLOTS // 2, 4, 2, N])
        k_raw = sb("k_raw", [128, K_SLOTS - 1, PIECE])
        w1_sb = k_raw[:, 0:2, :].rearrange("p a (b n) -> p (a b) n", n=H1)
        w2_sb = k_raw[:, 2].rearrange("p (b n) -> p b n", n=H2)
        z_sb = sb("z_sb", [128, Z_BLOCKS, N])
        h1_sb = sb("h1_sb", [128, H1_BLOCKS, N])
        k_slot = [k_raw[:, s, :] for s in range(K_SLOTS - 1)] + [h1_sb[:].rearrange("p b n -> p (b n)")]
        y_sb = h1_sb[0:1, 0, :]
        h2_sb = sb("h2_sb", [128, H2_BLOCKS, N])
        w3_sb = sb("w3_sb", [128, H2_BLOCKS])
        b1_sb = sb("b1_sb", [128, H1_BLOCKS])
        b2_sb = sb("b2_sb", [128, H2_BLOCKS])
        sel = sb("sel", [128, 94])
        ident = sb("ident", [128, 128])
        idx = sb("idx", [128, 2, 32], I32)

        t_ps = ctx.enter_context(nc.psum_tensor("t_ps", [128, T_SLOTS, 4, N], F32))
        z_ps = ctx.enter_context(nc.psum_tensor("z_ps", [128, Z_BANKS, 2, N], F32))
        e_ps = ctx.enter_context(nc.psum_tensor("e_ps", [128, 512], F32))
        mlp_ps = ctx.enter_context(nc.psum_tensor("mlp_ps", [128, 512], F32))

        ident_loaded = sem("ident_loaded")
        sel_loaded = sem("sel_loaded")
        mlp_weights_loaded = sem("mlp_weights_loaded")
        k_loaded = [sem(f"k_loaded{s}") for s in range(K_SLOTS)]
        k_rounded = sem("k_rounded")
        k_prepared = sem("k_prepared")
        k_prepared_pool = sem("k_prepared_pool")
        idx_loaded = [sem(f"idx_loaded{h}") for h in range(2)]
        first_idx_loaded = sem("first_idx_loaded")
        gathered = [sem(f"gathered{s}") for s in range(STAGE_SLOTS)]
        transposed = sem("transposed")
        upper_ready = sem("upper_ready")
        lower_ready = sem("lower_ready")
        moving_ready = sem("moving_ready")
        dense_loaded = [sem(f"dense_loaded{s}") for s in range(2)]
        half_formed = sem("half_formed")
        half_multiplied = sem("half_multiplied")
        items_summed = sem("items_summed")
        z_stored = sem("z_stored")
        mlp_formed = sem("mlp_formed")
        mlp_stored = sem("mlp_stored")
        y_written = sem("y_written")
        slots_granted = sem("slots_granted")

        def all_tiles(engine, tile):
            tile(0, True, False)
            with engine.Fori(1, TILES - 1) as t:
                tile(t, False, False)
            tile(TILES - 1, False, True)

        def wait_for_k(engine, piece):
            engine.wait_ge(k_prepared, piece + 1 - pool_prepares(piece))
            wait_count(engine, k_prepared_pool, pool_prepares(piece))

        def k_lower(tensor_tensor, prepared, piece):
            here, there = HALVES[piece % 2], HALVES[1 - piece % 2]
            cols = slice(piece * PIECE, (piece + 1) * PIECE)
            tensor_tensor(k_halves[there, cols], k_slot[piece // 2 % K_SLOTS][here],
                          k_halves[here, cols], ALU.subtract).then_inc(prepared, 1)

        block = ctx.enter_context(nc.Block())

        @block.gpsimd
        def _(pool):
            half_pairs = PHASES // 2

            def load_idx(t, half):
                for s in range(STAGE_SLOTS):
                    wait_count(pool, gathered[s], (t * 2 + half - 1) * 64)
                pool.dma_start(idx[:, half, :], ids[t, half]).then_inc(idx_loaded[half], 16)

            def tile(t, first, last):
                for p in range(PHASES):
                    half = p // half_pairs
                    if p % half_pairs == 0:
                        if first and half == 0:
                            pool.wait_ge(first_idx_loaded, 16)
                        else:
                            pool.wait_ge(idx_loaded[half], (t + half) * 16)
                    wait_count(pool, transposed, t * PHASES + p - STAGE_SLOTS + 1)
                    pool.sem_inc(slots_granted, 1)
                    for field in range(2):
                        for sub in range(SUBS):
                            column = (p % half_pairs) * 4 + 2 * field + sub
                            pool.indirect_dma_start(
                                stage[:, p % STAGE_SLOTS, sub, field * DIM:(field + 1) * DIM], None,
                                tables[2 * p + field],
                                bass.IndirectOffsetOnAxis(
                                    ap=idx[:, half, column:column + 1].bitcast(U32), axis=0),
                            ).then_inc(gathered[p % STAGE_SLOTS], 16)
                    if p == half_pairs - 1:
                        load_idx(t, 1)
                    if first:
                        for piece in K_POOL_AT.get(p, []):
                            pool.wait_ge(k_rounded, piece + 1)
                            k_lower(nc.gpsimd.tensor_tensor, k_prepared_pool, piece)
                    if p == PHASES - 1 and not last:
                        load_idx(t + 1, 0)

            all_tiles(pool, tile)

        @block.sync
        def _(sp):
            def load_k(load):
                if load >= K_SLOTS:
                    wait_for_k(sp, 2 * (load - K_SLOTS) + 1)
                partitions = 128 if 2 * load + 1 < PIECES else 64
                sp.dma_start(k_slot[load % K_SLOTS][0:partitions], kernel[load, 0:partitions]
                             ).then_inc(k_loaded[load % K_SLOTS], 16)

            def after_piece(piece):
                if piece % 2 and piece // 2 + K_SLOTS < K_LOADS:
                    load_k(piece // 2 + K_SLOTS)
                if piece == PIECES - 1:
                    wait_for_k(sp, piece)
                    for to, source in ((w1_sb, w1), (w2_sb, w2), (w3_sb[:], w3), (b1_sb[:], b1),
                                       (b2_sb[:], b2)):
                        sp.dma_start(to, source).then_inc(mlp_weights_loaded, 16)

            def load_dense(t, tail):
                i = TAIL_ITEM[tail]
                wait_count(sp, items_summed, t * ITEMS + i - PROD_SLOTS + 1)
                sp.dma_start(prod_slot(i)[DIM:DIM + 1, 2:4, :], dense[t, tail]
                             ).then_inc(dense_loaded[tail % 2], 16)

            def tile(t, first, last):
                for i in range(ITEMS):
                    if first:
                        for piece in K_LOWER_AT[i]:
                            after_piece(piece)
                    if i + 1 in TAIL_ITEM:
                        load_dense(t, TAIL_ITEM.index(i + 1))
                if not last:
                    load_dense(t + 1, 0)

            sp.dma_start(ident[:], ident_in).then_inc(ident_loaded, 16)
            load_k(0)
            load_k(1)
            sp.dma_start(sel[:], sel_in).then_inc(sel_loaded, 16)
            for load in range(2, K_SLOTS):
                load_k(load)
            load_dense(0, 0)
            for piece in K_LOWER_AT[-2] + K_LOWER_AT[-1]:
                after_piece(piece)
            all_tiles(sp, tile)

        @block.tensor
        def _(pe):
            def transpose_pair(t, p):
                g = t * PHASES + p
                uses = 2 * t + p // STAGE_SLOTS + 1
                pe.wait_ge(gathered[p % STAGE_SLOTS], uses * 64)
                wait_count(pe, upper_ready, g)
                for sub in range(SUBS):
                    last = nc.tensor.transpose(e_ps[:, sub * 128:(sub + 1) * 128],
                                               stage[:, p % STAGE_SLOTS, sub, :], ident[:])
                last.then_inc(transposed, 1)

            def form(t, i, first):
                item = ITEM_LIST[i]
                if first:
                    wait_for_k(pe, last_piece(i))
                pe.wait_ge(moving_ready, t * PHASES + item["m"] + 1)
                for q, (col, width, c) in enumerate(item["chunks"]):
                    if q % 2 == 0:
                        wait_count(pe, half_multiplied, 2 * (t * ITEMS + i - T_SLOTS) + q // 2 + 1)
                    for half in range(2):
                        last = nc.tensor.matmul(
                            t_ps[0:width, i % T_SLOTS, q, :], k_halves[:, col:col + width],
                            moving[:, (c // 2) % MOVING_SLOTS, c % 2, half, :],
                            start=(half == 0), stop=(half == 1))
                    if q % 2:
                        last.then_inc(half_formed, 1)

            def sum_two(t, i):
                bank, s = divmod(i, ITEMS_PER_BANK)
                selector = slice(30 - s, 62 - s)
                start, stop = s == 0, s == ITEMS_PER_BANK - 2
                two = prod[:, i // 2 % (PROD_SLOTS // 2)]
                pe.wait_ge(half_multiplied, 2 * (t * ITEMS + i + 2))
                tails = [ITEM_LIST[i + j]["tail"] for j in range(2)]
                for tail in tails:
                    if tail is not None:
                        pe.wait_ge(dense_loaded[tail % 2],
                                   (t * (len(TAIL_ITEM) // 2) + tail // 2 + 1) * 16)
                if start:
                    wait_count(pe, z_stored, (t - 1) * Z_BANKS + bank + 1)
                for q in range(4):
                    if q < 2 or tails == [None, None]:
                        last = nc.tensor.matmul(z_ps[32 * q:32 * q + 32, bank], sel[:, selector],
                                                two[:, q], start=start, stop=stop)
                        continue
                    out = z_ps[32 * q:32 * q + 32, bank]
                    if start:
                        nc.tensor.matmul(out.rearrange("p j (a n) -> p (j a) n", n=128), sel[:, 62:94],
                                         ident[:].unsqueeze(1).to_broadcast([128, 2 * SUBS, 128]),
                                         start=True, stop=False)
                    for j, tail in enumerate(tails):
                        rows = 128 if tail is None else DIM + 1
                        last = nc.tensor.matmul(out[:, j, :], sel[0:rows, selector],
                                                two[0:rows, q, j, :], start=False,
                                                stop=stop and j == 1)
                last.then_inc(items_summed, 2)

            def mlp_step(t, n, final=False):
                if n == 0:
                    pe.wait_ge(mlp_weights_loaded, 5 * 16)
                    pe.wait_ge(z_stored, (t + 1) * Z_BANKS - (1 if final else 0))
                elif final:
                    pe.wait_ge(mlp_stored, t * MLP_STEPS + n - 1)
                else:
                    pe.wait_ge(mlp_stored, t * MLP_STEPS + n)
                ps = e_ps if final and n % 2 else mlp_ps
                if n < H1_BLOCKS:
                    out, source, blocks = ps[:, 0:N], z_sb, Z_BLOCKS
                    weights = w1_sb[:, :, n * 128:(n + 1) * 128]
                elif n < MLP_STEPS - 1:
                    j = n - H1_BLOCKS
                    out, source, blocks = ps[:, 0:N], h1_sb, H1_BLOCKS
                    weights = w2_sb[:, :, j * 128:(j + 1) * 128]
                else:
                    out, source, blocks = ps[0:1, 0:N], h2_sb, H2_BLOCKS
                    weights = w3_sb[:].unsqueeze(2)
                for b in range(blocks):
                    if final and n == 0 and b == Z_BLOCKS - 2:
                        pe.wait_ge(z_stored, (t + 1) * Z_BANKS)
                    if final and n in (H1_BLOCKS, MLP_STEPS - 1) and b == blocks - 1:
                        pe.wait_ge(mlp_stored, t * MLP_STEPS + n)
                    last = nc.tensor.matmul(out, weights[:, b, :], source[:, b, :], start=(b == 0),
                                            stop=(b == blocks - 1))
                last.then_inc(mlp_formed, 1)

            def tile(t, first, last):
                for i in range(ITEMS + 1):
                    for ahead, p in (PREPARE_FIRST if first else PREPARE)[i]:
                        if not (last and ahead):
                            transpose_pair(t + ahead, p)
                    if i < ITEMS:
                        form(t, i, first)
                        if i == 0 and not first:
                            sum_two(t - 1, ITEMS - 2)
                        elif i % 2 and i > 1:
                            sum_two(t, i - SUM_LAG)
                        if i in MLP_AT and not first:
                            mlp_step(t - 1, MLP_AT[i])

            pe.wait_ge(ident_loaded, 16)
            for p in range(FIRST_EARLY):
                transpose_pair(0, p)
            pe.wait_ge(sel_loaded, 16)
            all_tiles(pe, tile)
            sum_two(TILES - 1, ITEMS - 2)
            pe.wait_ge(upper_ready, TILES * PHASES)
            for n in range(MLP_STEPS):
                mlp_step(TILES - 1, n, final=True)

        @block.vector
        def _(dve):
            def prepare_k(i):
                for piece in K_LOWER_AT[i]:
                    if piece not in POOL_PIECES:
                        dve.wait_ge(k_rounded, piece + 1)
                        k_lower(nc.vector.tensor_tensor, k_prepared, piece)

            def e_lower(t, p):
                dve.wait_ge(upper_ready, t * PHASES + p + 1)
                for field, here in enumerate(HALVES):
                    done = nc.vector.tensor_tensor(
                        moving[here, p % MOVING_SLOTS, field, 1, :], e_t[here, p, :],
                        moving[here, p % MOVING_SLOTS, field, 0, :], ALU.subtract)
                done.then_inc(lower_ready, 1)

            def multiply(t, i):
                item = ITEM_LIST[i]
                k, slot, target = item["k"], i % T_SLOTS, prod_slot(i)
                wait_count(dve, items_summed, t * ITEMS + i - PROD_SLOTS + 1)
                for h in range(2):
                    dve.wait_ge(half_formed, 2 * (t * ITEMS + i) + h + 1)
                    if h == 0 or item["tail"] is None:
                        nc.vector.tensor_tensor(
                            target[:, 2 * h:2 * h + 2, :], t_ps[:, slot, 2 * h:2 * h + 2, :],
                            e_t[:, k + h:k + h + 1, :].to_broadcast([128, 2, N]), ALU.mult
                        ).then_inc(half_multiplied, 1)
                    else:
                        nc.vector.tensor_tensor(
                            target[0:DIM, 2:4, :], t_ps[0:DIM, slot, 2:4, :], e_t[0:DIM, k:k + 2, :],
                            ALU.mult).then_inc(half_multiplied, 1)

            def prepare(t, i, first, last):
                for ahead, p in (PREPARE_FIRST if first else PREPARE)[i]:
                    if not (last and ahead):
                        e_lower(t + ahead, p)

            def tile(t, first, last):
                for i in range(ITEMS):
                    if first:
                        prepare(t, i, first, last)
                        prepare_k(i)
                    multiply(t, i)
                    if not first:
                        prepare(t, i, first, last)
                prepare(t, ITEMS, first, last)

            for p in range(FIRST_EARLY):
                prepare_k(p - FIRST_EARLY)
                e_lower(0, p)
            all_tiles(dve, tile)

        @block.scalar
        def _(act):
            def k_upper(piece):
                load = piece // 2
                act.wait_ge(k_loaded[load % K_SLOTS], (load // K_SLOTS + 1) * 16)
                here = HALVES[piece % 2]
                nc.scalar.copy(k_halves[here, piece * PIECE:(piece + 1) * PIECE],
                               k_slot[load % K_SLOTS][here]).then_inc(k_rounded, 1)

            def e_upper(t, p):
                act.wait_ge(transposed, t * PHASES + p + 1)
                if not isinstance(t, int) or t > 0:
                    act.wait_ge(half_multiplied, 2 * ((t - 1) * ITEMS + LAST_USE[p] + 1))
                nc.scalar.copy(e_t[:, p, :], e_ps[:, 0:N])
                before = t if p >= MOVING_SLOTS else t - 1
                wait_count(act, half_formed, 2 * (before * ITEMS + LAST_ITEM[p - MOVING_SLOTS] + 1))
                for field, here in enumerate(HALVES):
                    done = nc.scalar.copy(moving[here, p % MOVING_SLOTS, field, 0, :],
                                          e_ps[here, 0:N])
                done.then_inc(upper_ready, 1)

            def e_across(t, p):
                act.wait_ge(lower_ready, t * PHASES + p + 1)
                for field, here in enumerate(HALVES):
                    done = nc.scalar.copy(moving[HALVES[1 - field], p % MOVING_SLOTS, field],
                                          moving[here, p % MOVING_SLOTS, field])
                done.then_inc(moving_ready, 1)

            def store_z(t, bank):
                act.wait_ge(items_summed, t * ITEMS + (bank + 1) * ITEMS_PER_BANK)
                nc.scalar.copy(z_sb[:, 2 * bank:2 * bank + 2, :], z_ps[:, bank]).then_inc(z_stored, 1)

            def mlp_step(t, n, final=False):
                act.wait_ge(mlp_formed, t * MLP_STEPS + n + 1)
                ps = e_ps if final and n % 2 else mlp_ps
                if n < H1_BLOCKS:
                    nc.scalar.activation(h1_sb[:, n, :], ps[:, 0:N], ACT.Relu,
                                         bias=b1_sb[:, n:n + 1]).then_inc(mlp_stored, 1)
                elif n < MLP_STEPS - 1:
                    j = n - H1_BLOCKS
                    nc.scalar.activation(h2_sb[:, j, :], ps[:, 0:N], ACT.Relu,
                                         bias=b2_sb[:, j:j + 1]).then_inc(mlp_stored, 1)
                else:
                    nc.scalar.copy(y_sb, ps[0:1, 0:N]).then_inc(mlp_stored, 1)
                    act.wait_ge(mlp_stored, (t + 1) * MLP_STEPS)
                    act.dma_start(y_out[t], y_sb).then_inc(y_written, 16)

            def tile(t, first, last):
                def across(i):
                    for ahead, p in (PREPARE_FIRST if first else PREPARE)[i]:
                        if not (last and ahead):
                            e_across(t + ahead, p)

                for i in range(ITEMS + 1):
                    for ahead, p in (PREPARE_FIRST if first else PREPARE)[i]:
                        if not (last and ahead):
                            e_upper(t + ahead, p)
                    if first and i < ITEMS:
                        across(i)
                    bank, s = divmod(i - SUM_LAG + 1, ITEMS_PER_BANK)
                    if s == 0 and bank > 0:
                        store_z(t, bank - 1)
                    if i == ITEMS and not last:
                        store_z(t, Z_BANKS - 1)
                    if i > 0 and not first:
                        across(i - 1)
                    if first and i < ITEMS:
                        for piece in K_UPPER_AT[i]:
                            k_upper(piece)
                    if i in MLP_AT and not first:
                        mlp_step(t - 1, MLP_AT[i])
                across(ITEMS)
                if not first:
                    act.wait_ge(y_written, t * 16)

            act.dma_start(idx[:, 0, :], ids[0, 0]).then_inc(first_idx_loaded, 16)
            for p in range(FIRST_EARLY):
                for piece in K_UPPER_AT[p - FIRST_EARLY]:
                    k_upper(piece)
                e_upper(0, p)
                e_across(0, p)
            all_tiles(act, tile)
            store_z(TILES - 1, Z_BANKS - 1)
            for n in range(MLP_STEPS):
                mlp_step(TILES - 1, n, final=True)
            act.wait_ge(y_written, TILES * 16)


def kernel(**inputs):
    import concourse.bacc as bacc
    from concourse.bass_utils import run_bass_kernel_spmd

    nc = bacc.Bacc("TRN2", target_bir_lowering=False, num_devices=1)
    arrays = {}

    def give(name, array):
        array = np.ascontiguousarray(array)
        arrays[name] = array
        return nc.dram_tensor(name, array.shape, mybir.dt.from_np(array.dtype),
                              kind="ExternalInput").ap()

    ids = np.asarray(inputs["ids"]).reshape(TILES, SUBS, 128, 2, PHASES // 2, 2)
    ids = give("ids_in", ids.transpose(0, 3, 2, 4, 5, 1).reshape(TILES, 2, 128, 32))
    tables = [give(f"table_{f}", inputs[f"tbl_{f}"]) for f in range(FIELDS)]
    k = np.asarray(inputs["L0_rec_kernel"])[:, K_ORDER, :].reshape(DIM, PIECES, PIECE)
    k = np.concatenate([k, k[:, :2 * K_LOADS - PIECES]], axis=1).transpose(1, 0, 2)
    k = give("kernel_in", k.reshape(K_LOADS, 2 * DIM, PIECE))
    w1 = give("w1_in", np.asarray(inputs["W_top1"])[Z_ROWS].reshape(Z_BLOCKS, 128, H1).transpose(1, 0, 2))
    b1 = give("b1_in", np.asarray(inputs["b_top1"]).reshape(H1_BLOCKS, 128).T)
    w2 = give("w2_in", np.asarray(inputs["W_top2"]).reshape(H1_BLOCKS, 128, H2).transpose(1, 0, 2))
    b2 = give("b2_in", np.asarray(inputs["b_top2"]).reshape(H2_BLOCKS, 128).T)
    w3 = give("w3_in", np.asarray(inputs["W_top3"]).reshape(H2_BLOCKS, 128).T)
    dense = np.asarray(inputs["dense_ctx"]).reshape(TILES, N, DENSE // 2, 2)
    dense = give("dense_in", dense.transpose(0, 2, 3, 1).reshape(TILES, DENSE // 2, 1, 2, N))
    sel = np.zeros((128, 94), np.float32)
    sel[0:64, 30] = 1.0
    sel[64:128, 31] = 1.0
    sel = give("sel_in", sel)
    ident = give("ident_in", np.eye(128, dtype=np.float32))
    y = nc.dram_tensor("y_out", (TILES, 1, N), F32, kind="ExternalOutput").ap()
    dlrm_tower(nc, ids, tables, k, w1, b1, w2, b2, w3, dense, sel, ident, y)
    result = run_bass_kernel_spmd(nc, [arrays], core_ids=[0])
    return result.results[0]["y_out"].reshape(BATCH, 1)
```
